# Optimizing a Trainium2 kernel written in Bass

```python
import numpy as np
import jax
import jax.numpy as jnp

def _softmax(x, axis=-1):
    return jax.nn.softmax(x, axis=axis)

def _gelu(x):
    return jax.nn.gelu(x, approximate=True)

def _silu(x):
    return jax.nn.silu(x)

def _sigmoid(x):
    return jax.nn.sigmoid(x)

def _layernorm(x, axis=-1, eps=1e-05):
    m = jnp.mean(x, axis=axis, keepdims=True)
    v = jnp.var(x, axis=axis, keepdims=True)
    return (x - m) / jnp.sqrt(v + eps)

def _scatter_add(tgt, idx, src, axis=0):
    return tgt.at[idx].add(src)

def _segment_sum(src, seg, n):
    return jax.ops.segment_sum(src, seg, n)
kernel_name = 'mk_adj_resnorm_d1_adj_r2_8ee04b'

def setup_inputs(seed: int=0):
    np.random.seed(seed)
    _w = jnp.asarray

    def _rec_inputs():
        import jax
        import jax.numpy as jnp
        _gk = jax.random.key(seed)
        x = 7.22e-05 + 1 * jax.random.normal(jax.random.fold_in(_gk, 1), (128, 128, 256), jnp.float32)
        _a = jax.random.bernoulli(jax.random.fold_in(_gk, 2), 0.0625, (128, 128))
        _a = jnp.logical_or(_a, jnp.swapaxes(_a, -1, -2))
        _a = jnp.logical_or(_a, jnp.eye(128, dtype=bool))
        _af = _a.astype(jnp.float32)
        _af = _af * jax.random.uniform(jax.random.fold_in(_gk, 3), (128, 128), jnp.float32, 0.05, 0.00390622)
        adj = _af
        return (x, adj)
    x, adj = _rec_inputs()

    def _L0_gnn_setup():
        import jax, jax.numpy as jnp
        import numpy as np
        B, N, D, T = (64, 128, 256, 3)

        def _lin(v, W, b):
            return jnp.einsum('...i,oi->...o', v, W) + b
        key = jax.random.key(seed)
        ks = jax.random.split(key, 12)
        s2 = 1.0 / np.sqrt(2 * D)
        s1 = 1.0 / np.sqrt(D)
        return {'x': jax.random.normal(ks[0], (B, N, D), jnp.float32), 'in_mat': jax.random.uniform(ks[1], (N, N), jnp.float32) / N, 'out_mat': jax.random.uniform(ks[2], (N, N), jnp.float32) / N, 'w3_w': jax.random.normal(ks[3], (D, 2 * D), jnp.float32) * s2, 'w3_b': jnp.zeros((D,), jnp.float32), 'u3_w': jax.random.normal(ks[4], (D, D), jnp.float32) * s1, 'u3_b': jnp.zeros((D,), jnp.float32), 'w4_w': jax.random.normal(ks[5], (D, 2 * D), jnp.float32) * s2, 'w4_b': jnp.zeros((D,), jnp.float32), 'w5_w': jax.random.normal(ks[6], (D, 2 * D), jnp.float32) * s2, 'w5_b': jnp.zeros((D,), jnp.float32), 'u5_w': jax.random.normal(ks[7], (D, D), jnp.float32) * s1, 'u5_b': jnp.zeros((D,), jnp.float32)}
    _L0_gnn_all = _L0_gnn_setup()
    _L0_gnn_in = {k: v for k, v in _L0_gnn_all.items() if k in ('w3_w', 'w3_b', 'u3_w', 'u3_b', 'w4_w', 'w4_b', 'w5_w', 'w5_b', 'u5_w', 'u5_b')}
    del _L0_gnn_all
    return {'x': x, 'adj': adj, 'L0_gnn_w3_w': _L0_gnn_in['w3_w'], 'L0_gnn_w3_b': _L0_gnn_in['w3_b'], 'L0_gnn_u3_w': _L0_gnn_in['u3_w'], 'L0_gnn_u3_b': _L0_gnn_in['u3_b'], 'L0_gnn_w4_w': _L0_gnn_in['w4_w'], 'L0_gnn_w4_b': _L0_gnn_in['w4_b'], 'L0_gnn_w5_w': _L0_gnn_in['w5_w'], 'L0_gnn_w5_b': _L0_gnn_in['w5_b'], 'L0_gnn_u5_w': _L0_gnn_in['u5_w'], 'L0_gnn_u5_b': _L0_gnn_in['u5_b']}

def reference(x, adj, L0_gnn_w3_w, L0_gnn_w3_b, L0_gnn_u3_w, L0_gnn_u3_b, L0_gnn_w4_w, L0_gnn_w4_b, L0_gnn_w5_w, L0_gnn_w5_b, L0_gnn_u5_w, L0_gnn_u5_b):
    import jax
    import jax.numpy as jnp

    def _L0_gnn_ref(x, in_mat, out_mat, w3_w, w3_b, u3_w, u3_b, w4_w, w4_b, w5_w, w5_b, u5_w, u5_b):
        import jax, jax.numpy as jnp
        import numpy as np
        B, N, D, T = (64, 128, 256, 3)

        def _lin(v, W, b):
            return jnp.einsum('...i,oi->...o', v, W) + b
        h = x
        for _ in range(T):
            a_in = jnp.einsum('nm,bmd->bnd', in_mat, h)
            a_out = jnp.einsum('nm,bmd->bnd', out_mat, h)
            av = jnp.concatenate([a_in, a_out], axis=-1)
            z = jax.nn.sigmoid(_lin(av, w3_w, w3_b) + _lin(h, u3_w, u3_b))
            r = jax.nn.sigmoid(_lin(av, w4_w, w4_b) + _lin(h, u3_w, u3_b))
            hv = jnp.tanh(_lin(av, w5_w, w5_b) + _lin(r * h, u5_w, u5_b))
            h = (1.0 - z) * h + z * hv
        return h
    x = _layernorm(x + _L0_gnn_ref(x, adj, adj, L0_gnn_w3_w, L0_gnn_w3_b, L0_gnn_u3_w, L0_gnn_u3_b, L0_gnn_w4_w, L0_gnn_w4_b, L0_gnn_w5_w, L0_gnn_w5_b, L0_gnn_u5_w, L0_gnn_u5_b), axis=-1)
    return x

_drawn_inputs = setup_inputs


def setup_inputs(seed=0):
    import zlib

    import numpy as np

    out = dict(_drawn_inputs(seed))
    spreads = {'L0_gnn_w3_b': (0.0, 0.456),
     'L0_gnn_u3_b': (0.0, 0.402),
     'L0_gnn_w4_b': (0.0, 0.8),
     'L0_gnn_w5_b': (0.0, 0.1),
     'L0_gnn_u5_b': (0.0, 0.1)}
    factors = {'L0_gnn_w4_w': 5.05}
    for name, (base, spread) in spreads.items():
        noise = np.random.default_rng([zlib.crc32(name.encode()), seed]).standard_normal(out[name].shape)
        drawn = base * np.exp(spread * noise) if base else spread * noise
        out[name] = jnp.asarray(drawn.astype(out[name].dtype))
    for name, factor in factors.items():
        out[name] = (out[name] * factor).astype(out[name].dtype)
    return out
```

```python
from contextlib import ExitStack

import concourse.bass as bass
from concourse import mybir

P = 128
F32 = mybir.dt.float32
F32R = mybir.dt.float32r
ALU = mybir.AluOpType
ACT = mybir.ActivationFunctionType

T = 3
GB = 4
EPS = 1e-5


def gated_graph_kernel(nc, x_tok, x_feat, adj_t, w3_t, w4_t, w5_t, u3_t, u5_t, biases, out):
    GROUPS = x_tok.shape[0]
    N = adj_t.shape[0]
    D = x_tok.shape[2] // GB
    C = D // P
    TOK = GB * N
    assert N == P and C == 2 and TOK == 512
    STREAMS = 2
    ITERS = GROUPS // STREAMS
    SLOTS = STREAMS * T
    REG = STREAMS * (T - 1)
    PASSES = ((0, 0), (0, 1), (1, 0))

    with ExitStack() as ctx:
        def sb(name, shape, dt=F32):
            return ctx.enter_context(nc.sbuf_tensor(name, shape, dt))

        def sem(name):
            return ctx.enter_context(nc.semaphore(name))

        raw_adj = sb("raw_adj", [P, N])
        adj = sb("adj", [P, 2, N], F32R)
        raw = {n: sb(f"raw_{n}", [P, 2 * C, D]) for n in ("w3", "w4", "w5")}
        raw |= {n: sb(f"raw_{n}", [P, C, D]) for n in ("u3", "u5")}
        wt = {n: sb(f"{n}_parts", [P, 2, C, D], F32R) for n in ("u3", "w4", "w3", "w5", "u5")}
        bias_in = sb("bias_in", [P, 5, C])
        gate_bias = sb("gate_bias", [P, 3, C])
        ident = sb("ident", [P, P])
        minus_half = sb("minus_half", [P, GB])
        eps = sb("eps", [P, GB])

        x_in = [sb(f"x_in{s}", [P, GB, D]) for s in range(STREAMS)]
        tok = [sb(f"tok{s}", [P, 2, GB, D], F32R) for s in range(STREAMS)]
        h0 = [sb(f"h0_{s}", [P, C, TOK]) for s in range(STREAMS)]
        h = [sb(f"h{s}", [P, C, TOK]) for s in range(STREAMS)]
        feat = [sb(f"feat{s}", [P, 2, C, TOK], F32R) for s in range(STREAMS)]
        y = [sb(f"y{s}", [P, GB, D]) for s in range(STREAMS)]
        stats = [sb(f"stats{s}", [P, GB, 6]) for s in range(STREAMS)]
        mean_var = [sb(f"mean_var{s}", [P, GB, 2]) for s in range(STREAMS)]
        rstd = [sb(f"rstd{s}", [P, GB]) for s in range(STREAMS)]

        a = sb("a", [P, 2, C, TOK], F32R)
        u = sb("u", [P, C, TOK])
        r = sb("r", [P, C, TOK])
        rh = sb("rh", [P, 2, C, TOK], F32R)
        z = sb("z", [P, C, TOK])
        cand = sb("cand", [P, C, TOK])

        ps_a = ctx.enter_context(nc.psum_tensor("ps_a", [P, C, TOK], F32))
        ps_r = ctx.enter_context(nc.psum_tensor("ps_r", [P, C, TOK], F32))
        ps_z = ctx.enter_context(nc.psum_tensor("ps_z", [P, C, TOK], F32))
        ps_c = ctx.enter_context(nc.psum_tensor("ps_c", [P, C, TOK], F32))

        adj_in = sem("adj_in")
        w_in = {n: sem(f"{n}_in") for n in ("u3", "w4", "w3", "w5", "u5")}
        b_in = sem("b_in")
        x_loaded = [sem(f"x_loaded{s}") for s in range(STREAMS)]
        h0_loaded = [sem(f"h0_loaded{s}") for s in range(STREAMS)]
        stored = [sem(f"stored{s}") for s in range(STREAMS)]
        w_ready = sem("w_ready")
        w_chain = sem("w_chain")
        bias_ready = sem("bias_ready")
        ident_zero = sem("ident_zero")
        ident_ready = sem("ident_ready")
        a_done = sem("a_done")
        u_done = sem("u_done")
        r_done = sem("r_done")
        z_done = sem("z_done")
        t_done = sem("t_done")
        c_done = sem("c_done")
        tanh_done = sem("tanh_done")
        a_hi_done = sem("a_hi_done")
        u_copied = sem("u_copied")
        r_sig = sem("r_sig")
        rh_hi_done = sem("rh_hi_done")
        z_sig = sem("z_sig")
        feat_hi_done = sem("feat_hi_done")
        tok_hi_done = sem("tok_hi_done")
        y_copied = sem("y_copied")
        x_hi_done = sem("x_hi_done")
        h0_hi_done = sem("h0_hi_done")
        a_lo_done = sem("a_lo_done")
        rh_done = sem("rh_done")
        rh_lo_done = sem("rh_lo_done")
        z_added = sem("z_added")
        diff_done = sem("diff_done")
        step_done = sem("step_done")
        h_done = sem("h_done")
        feat_lo_done = sem("feat_lo_done")
        tok_lo_done = sem("tok_lo_done")
        x_lo_done = sem("x_lo_done")
        h0_lo_done = sem("h0_lo_done")
        last_h = sem("last_h")
        stats_done = sem("stats_done")
        var_ready = sem("var_ready")
        var_eps = sem("var_eps")
        rstd_ready = sem("rstd_ready")
        norm_done = sem("norm_done")

        def by_slot(i, k, c):
            return i * (C * SLOTS) + (C * k + c + 1)

        def once_by_slot(i, k):
            return i * SLOTS + (k + 1)

        def by_fed(i, k, c):
            return i * (C * REG) + (C * k + c + 1)

        def by_group(i, s, each=1):
            return i * (STREAMS * each) + each * (s + 1)

        def before(i, k):
            if k:
                return i, k - 1
            return None if isinstance(i, int) and i == 0 else (i - 1, SLOTS - 1)

        def two_before(i, k):
            q = before(i, k)
            return q and before(*q)

        def where(k):
            return k % STREAMS, k // STREAMS

        def h_of(k):
            s, t = where(k)
            return h0[s] if t == 0 else h[s]

        block = ctx.enter_context(nc.Block())

        @block.sync
        def _(sp):
            def load_x(g, s):
                sp.dma_start(x_in[s][:, :, :], x_tok[g].rearrange("p (b d) -> p b d", b=GB)
                             ).then_inc(x_loaded[s], 16)

            def load_h0(g, s):
                sp.dma_start(h0[s][:, :, :], x_feat[g].rearrange("p (c t) -> p c t", c=C)
                             ).then_inc(h0_loaded[s], 16)

            def store_y(i, s):
                sp.wait_ge(norm_done, by_group(i, s))
                sp.dma_start(out[i * STREAMS + s].rearrange("p (b d) -> p b d", b=GB), y[s][:, :, :]
                             ).then_inc(stored[s], 16)

            def iteration(i, first, last):
                if not first:
                    sp.wait_ge(h_done, i * SLOTS)
                    load_h0(i * STREAMS + 1, 1)
                    store_y(i - 1, 0)
                    store_y(i - 1, 1)
                if not last:
                    for s in range(STREAMS):
                        sp.wait_ge(x_lo_done, by_group(i, s))
                        load_x((i + 1) * STREAMS + s, s)
                    sp.wait_ge(h_done, once_by_slot(i, SLOTS - 2))
                    load_h0((i + 1) * STREAMS, 0)

            sp.dma_start(raw_adj[:, :], adj_t).then_inc(adj_in, 16)
            load_x(0, 0)
            load_h0(0, 0)
            sp.dma_start(raw["w4"][:, :, :], w4_t.rearrange("p (c o) -> p c o", o=D)).then_inc(w_in["w4"], 16)
            sp.dma_start(raw["w5"][:, :, :], w5_t.rearrange("p (c o) -> p c o", o=D)).then_inc(w_in["w5"], 16)
            load_x(1, 1)
            load_h0(1, 1)
            iteration(0, True, False)
            with sp.Fori(1, ITERS - 1) as i:
                iteration(i, False, False)
            iteration(ITERS - 1, False, True)
            for s in range(STREAMS):
                store_y(ITERS - 1, s)
            for s in range(STREAMS):
                sp.wait_ge(stored[s], 16 * ITERS)

        @block.tensor
        def _(pe):
            def gate(ps, o, name, parts, begin, end, k_first=0):
                last = None
                for c in range(C):
                    for n, (w, d) in enumerate(PASSES):
                        last = pe.matmul(ps[:, o, :], wt[name][:, w, c, o * P:(o + 1) * P],
                                         parts[:, d, c, :],
                                         start=begin and c == 0 and n == 0,
                                         stop=end and c == C - 1 and n == len(PASSES) - 1,
                                         skip_group_check=True)
                return last

            def transpose_result(q):
                qi, qk = q
                s, _ = where(qk)
                pe.wait_ge(h_done, once_by_slot(qi, qk))
                for j in range(2):
                    for b in range(GB // 2 * j, GB // 2 * (j + 1)):
                        for c in range(C):
                            col = (b % (GB // 2)) * D + c * P
                            last = pe.transpose(ps_a[:, j, col:col + P], h[s][:, c, b * N:(b + 1) * N],
                                                ident[:, :])
                    last.then_inc(t_done, 1)

            def slot(i, k, first, last):
                s, t = where(k)
                start_up = first and k == 0
                if t == 0:
                    if not first:
                        pe.wait_ge(y_copied, by_group(i - 1, s, C))
                    pe.wait_ge(x_lo_done, by_group(i, s))
                else:
                    pe.wait_ge(tok_lo_done, by_fed(i, k - STREAMS, 1))
                if start_up:
                    pe.wait_ge(w_ready, 1)
                for c in range(C):
                    for b in range(GB):
                        for n, (d, w) in enumerate(PASSES):
                            mm = pe.matmul(ps_a[:, c, b * N:(b + 1) * N], tok[s][:, d, b, c * P:(c + 1) * P],
                                           adj[:, w, :], start=n == 0, stop=n == len(PASSES) - 1)
                    mm.then_inc(a_done, 1)
                if t == 0:
                    pe.wait_ge(h0_lo_done, by_group(i, s))
                else:
                    pe.wait_ge(feat_lo_done, by_fed(i, k - STREAMS, 1))
                if start_up:
                    pe.wait_ge(w_ready, 2)
                for o in range(C):
                    if not start_up:
                        pe.wait_ge(r_sig, by_slot(*before(i, k), o))
                    gate(ps_r, o, "u3", feat[s], True, False).then_inc(u_done, 1)
                pe.wait_ge(a_lo_done, by_slot(i, k, 1))
                if start_up:
                    pe.wait_ge(w_ready, 3)
                for o in range(C):
                    pe.wait_ge(u_copied, by_slot(i, k, o))
                    gate(ps_r, o, "w4", a, False, True).then_inc(r_done, 1)
                if start_up:
                    pe.wait_ge(w_ready, 4)
                for o in range(C):
                    if not start_up:
                        pe.wait_ge(z_sig, by_slot(*before(i, k), o))
                    gate(ps_z, o, "w3", a, True, True).then_inc(z_done, 1)
                if not start_up:
                    transpose_result(before(i, k))
                if start_up:
                    pe.wait_ge(w_ready, 5)
                for o in range(C):
                    if not start_up:
                        pe.wait_ge(tanh_done, by_slot(*before(i, k), o))
                    gate(ps_c, o, "w5", a, True, False)
                if start_up:
                    pe.wait_ge(w_ready, 6)
                pe.wait_ge(rh_lo_done, by_slot(i, k, 1))
                for o in range(C):
                    gate(ps_c, o, "u5", rh, False, True).then_inc(c_done, 1)

            pe.wait_ge(ident_ready, 1)
            for k in range(SLOTS):
                slot(0, k, True, False)
            with pe.Fori(1, ITERS - 1) as i:
                for k in range(SLOTS):
                    slot(i, k, False, False)
            for k in range(SLOTS):
                slot(ITERS - 1, k, False, True)
            transpose_result((ITERS - 1, SLOTS - 1))

        @block.scalar
        def _(act):
            def tanh(q):
                qi, qk = q
                for o in range(C):
                    act.wait_ge(c_done, by_slot(qi, qk, o))
                    nc.scalar.activation(cand[:, o, :], ps_c[:, o, :], ACT.Tanh,
                                         bias=gate_bias[:, 2, o:o + 1]).then_inc(tanh_done, 1)

            def copy_y(q):
                qi, qk = q
                s, _ = where(qk)
                if not (isinstance(qi, int) and qi == 0):
                    act.wait_ge(stored[s], qi * 16)
                for j in range(2):
                    act.wait_ge(t_done, by_slot(qi, qk, j))
                    half = slice(GB // 2 * j, GB // 2 * (j + 1))
                    nc.scalar.activation(y[s][:, half, :], ps_a[:, j, :].rearrange("p (b d) -> p b d", d=D),
                                         ACT.Copy).then_inc(y_copied, 1)

            def split_x(i, s):
                act.wait_ge(x_loaded[s], i * 16 + 16)
                nc.scalar.activation(tok[s][:, 0, :, :], x_in[s][:, :, :], ACT.Copy).then_inc(x_hi_done, 1)

            def split_h0(i, s):
                act.wait_ge(h0_loaded[s], i * 16 + 16)
                nc.scalar.activation(feat[s][:, 0, :, :], h0[s][:, :, :], ACT.Copy).then_inc(h0_hi_done, 1)

            def slot(i, k, first, last):
                q = before(i, k)
                if q:
                    tanh(q)
                    qs, qt = where(q[1])
                for c in range(C):
                    act.wait_ge(a_done, by_slot(i, k, c))
                    nc.scalar.activation(a[:, 0, c, :], ps_a[:, c, :], ACT.Copy).then_inc(a_hi_done, 1)
                for o in range(C):
                    act.wait_ge(u_done, by_slot(i, k, o))
                    nc.scalar.activation(u[:, o, :], ps_r[:, o, :], ACT.Copy).then_inc(u_copied, 1)
                if q:
                    act.wait_ge(rh_lo_done, by_slot(*q, 1))
                for o in range(C):
                    act.wait_ge(r_done, by_slot(i, k, o))
                    nc.scalar.activation(r[:, o, :], ps_r[:, o, :], ACT.Sigmoid,
                                         bias=gate_bias[:, 1, o:o + 1]).then_inc(r_sig, 1)
                    if q:
                        act.wait_ge(h_done, once_by_slot(*q))
                        if qt < T - 1:
                            nc.scalar.activation(feat[qs][:, 0, o, :], h[qs][:, o, :], ACT.Copy
                                                 ).then_inc(feat_hi_done, 1)
                for c in range(C):
                    act.wait_ge(rh_done, by_slot(i, k, c))
                    nc.scalar.activation(rh[:, 0, c, :], r[:, c, :], ACT.Copy).then_inc(rh_hi_done, 1)
                for o in range(C):
                    act.wait_ge(z_added, by_slot(i, k, o))
                    nc.scalar.activation(z[:, o, :], ps_z[:, o, :], ACT.Sigmoid,
                                         bias=gate_bias[:, 0, o:o + 1]).then_inc(z_sig, 1)
                if q and qt < T - 1:
                    for j in range(2):
                        act.wait_ge(t_done, by_slot(*q, j))
                        half = slice(GB // 2 * j, GB // 2 * (j + 1))
                        nc.scalar.activation(tok[qs][:, 0, half, :],
                                             ps_a[:, j, :].rearrange("p (b d) -> p b d", d=D), ACT.Copy
                                             ).then_inc(tok_hi_done, 1)
                elif q:
                    copy_y(q)
                if k == SLOTS - 2 and not last:
                    split_x(i + 1, 0)
                if k == SLOTS - 1 and not last:
                    split_x(i + 1, 1)
                    split_h0(i + 1, 0)
                if k == 0 and not first:
                    split_h0(i, 1)

            act.dma_start(raw["u3"][:, :, :], u3_t.rearrange("p (c o) -> p c o", o=D)).then_inc(w_in["u3"], 16)
            act.dma_start(bias_in[:, :, :], biases.rearrange("p (n c) -> p n c", c=C)).then_inc(b_in, 16)
            act.dma_start(raw["w3"][:, :, :], w3_t.rearrange("p (c o) -> p c o", o=D)).then_inc(w_in["w3"], 16)
            act.dma_start(raw["u5"][:, :, :], u5_t.rearrange("p (c o) -> p c o", o=D)).then_inc(w_in["u5"], 16)
            for s in range(STREAMS):
                split_x(0, s)
                split_h0(0, s)
            act.wait_ge(bias_ready, 1)
            for k in range(SLOTS):
                slot(0, k, True, False)
            with act.Fori(1, ITERS - 1) as i:
                for k in range(SLOTS):
                    slot(i, k, False, False)
            for k in range(SLOTS):
                slot(ITERS - 1, k, False, True)
            tanh((ITERS - 1, SLOTS - 1))
            copy_y((ITERS - 1, SLOTS - 1))

        @block.vector
        def _(dve):
            def lo(out_, full, hi):
                return nc.vector.tensor_tensor(out_, full, hi.bitcast(F32), ALU.subtract)

            chain = [0]

            def link(ins):
                chain[0] += 1
                ins.then_inc(w_chain, 1)
                dve.wait_ge(w_chain, chain[0])

            def prepare(name):
                dve.wait_ge(w_in[name], 16)
                w = raw[name]
                if name[0] == "w":
                    link(nc.vector.tensor_tensor(w[:, 0:C, :], w[:, 0:C, :], w[:, C:2 * C, :], ALU.add))
                link(nc.vector.tensor_copy(wt[name][:, 0, :, :], w[:, 0:C, :]))
                lo(wt[name][:, 1, :, :], w[:, 0:C, :], wt[name][:, 0, :, :]).then_inc(w_ready, 1)

            def split_x(i, s):
                dve.wait_ge(x_hi_done, by_group(i, s))
                lo(tok[s][:, 1, :, :], x_in[s][:, :, :], tok[s][:, 0, :, :]).then_inc(x_lo_done, 1)

            def split_h0(i, s):
                dve.wait_ge(h0_hi_done, by_group(i, s))
                lo(feat[s][:, 1, :, :], h0[s][:, :, :], feat[s][:, 0, :, :]).then_inc(h0_lo_done, 1)

            def diff(q):
                dve.wait_ge(tanh_done, by_slot(*q, 1))
                nc.vector.tensor_tensor(cand[:, :, :], cand[:, :, :], h_of(q[1])[:, :, :], ALU.subtract
                                        ).then_inc(diff_done, 1)

            def scale_by_z(q):
                dve.wait_ge(z_sig, by_slot(*q, 1))
                dve.wait_ge(diff_done, once_by_slot(*q))
                nc.vector.tensor_tensor(cand[:, :, :], cand[:, :, :], z[:, :, :], ALU.mult
                                        ).then_inc(step_done, 1)

            def new_h(q):
                qi, qk = q
                s, t = where(qk)
                dve.wait_ge(step_done, once_by_slot(*q))
                ins = nc.vector.tensor_tensor(h[s][:, :, :], cand[:, :, :], h_of(qk)[:, :, :], ALU.add)
                if t == T - 1:
                    ins.then_inc(last_h, 1)
                    dve.wait_ge(last_h, by_group(qi, s))
                    ins = nc.vector.tensor_tensor(h[s][:, :, :], h[s][:, :, :], h0[s][:, :, :], ALU.add)
                ins.then_inc(h_done, 1)

            def norm_stats(i, s):
                dve.wait_ge(y_copied, by_group(i, s, C))
                for b in range(GB):
                    ins = nc.vector.bn_stats(stats[s][:, b, :], y[s][:, b, :])
                ins.then_inc(stats_done, 1)

            def mean_and_var(i, s):
                for b in range(GB):
                    ins = nc.vector.bn_aggr(mean_var[s][:, b, :], stats[s][:, b, :])
                ins.then_inc(var_ready, 1)

            def normalise(i, s):
                dve.wait_ge(rstd_ready, by_group(i, s))
                for b in range(GB):
                    ins = nc.vector.tensor_scalar(y[s][:, b, :], y[s][:, b, :], mean_var[s][:, b, 0:1],
                                                  rstd[s][:, b:b + 1], ALU.subtract, ALU.mult)
                ins.then_inc(norm_done, 1)

            def slot(i, k, first, last):
                s, _ = where(k)
                q = before(i, k)
                if q:
                    if k < STREAMS and not first:
                        dve.wait_ge(stats_done, by_group(i - 1, k))
                    diff(q)
                    qs, qt = where(q[1])
                    if k < STREAMS and not first:
                        mean_and_var(i - 1, k)
                for c in range(C):
                    dve.wait_ge(a_hi_done, by_slot(i, k, c))
                    lo(a[:, 1, c, :], ps_a[:, c, :], a[:, 0, c, :]).then_inc(a_lo_done, 1)
                    if q and c == 0:
                        scale_by_z(q)
                if q:
                    new_h(q)
                for c in range(C):
                    dve.wait_ge(r_sig, by_slot(i, k, c))
                    nc.vector.tensor_tensor(r[:, c, :], r[:, c, :], h_of(k)[:, c, :], ALU.mult
                                            ).then_inc(rh_done, 1)
                if q and qt < T - 1:
                    for c in range(C):
                        dve.wait_ge(feat_hi_done, by_fed(*q, c))
                        lo(feat[qs][:, 1, c, :], h[qs][:, c, :], feat[qs][:, 0, c, :]).then_inc(feat_lo_done, 1)
                for c in range(C):
                    dve.wait_ge(rh_hi_done, by_slot(i, k, c))
                    lo(rh[:, 1, c, :], r[:, c, :], rh[:, 0, c, :]).then_inc(rh_lo_done, 1)
                if k == 0 and not first:
                    normalise(i - 1, 0)
                if k == 1 and not first:
                    normalise(i - 1, 1)
                for o in range(C):
                    dve.wait_ge(z_done, by_slot(i, k, o))
                    dve.wait_ge(u_copied, by_slot(i, k, o))
                    nc.vector.tensor_tensor(ps_z[:, o, :], ps_z[:, o, :], u[:, o, :], ALU.add
                                            ).then_inc(z_added, 1)
                if q and qt < T - 1:
                    for j in range(2):
                        dve.wait_ge(tok_hi_done, by_fed(*q, j))
                        half = slice(GB // 2 * j, GB // 2 * (j + 1))
                        lo(tok[qs][:, 1, half, :], ps_a[:, j, :].rearrange("p (b d) -> p b d", d=D),
                           tok[qs][:, 0, half, :]).then_inc(tok_lo_done, 1)
                if k == SLOTS - 2 and not last:
                    split_x(i + 1, 0)
                if k == SLOTS - 1:
                    if not last:
                        split_x(i + 1, 1)
                        split_h0(i + 1, 0)
                    norm_stats(i, 0)
                if k == 0 and not first:
                    split_h0(i, 1)
                    norm_stats(i - 1, 1)

            dve.wait_ge(adj_in, 16)
            link(nc.vector.tensor_copy(adj[:, 0, :], raw_adj[:, :]))
            lo(adj[:, 1, :], raw_adj[:, :], adj[:, 0, :]).then_inc(w_ready, 1)
            split_x(0, 0)
            prepare("u3")
            split_h0(0, 0)
            prepare("w4")
            dve.wait_ge(b_in, 16)
            for n, other in ((0, 3), (1, 3), (2, 4)):
                ins = nc.vector.tensor_tensor(gate_bias[:, n, :], bias_in[:, n, :], bias_in[:, other, :], ALU.add)
            ins.then_inc(bias_ready, 1)
            prepare("w3")
            prepare("w5")
            prepare("u5")
            split_x(0, 1)
            split_h0(0, 1)
            for k in range(SLOTS):
                slot(0, k, True, False)
            with dve.Fori(1, ITERS - 1) as i:
                for k in range(SLOTS):
                    slot(i, k, False, False)
            for k in range(SLOTS):
                slot(ITERS - 1, k, False, True)
            end = (ITERS - 1, SLOTS - 1)
            dve.wait_ge(stats_done, by_group(ITERS - 1, 0))
            mean_and_var(ITERS - 1, 0)
            diff(end)
            scale_by_z(end)
            new_h(end)
            normalise(ITERS - 1, 0)
            norm_stats(ITERS - 1, 1)
            dve.wait_ge(stats_done, by_group(ITERS - 1, 1))
            mean_and_var(ITERS - 1, 1)
            normalise(ITERS - 1, 1)

        @block.gpsimd
        def _(pool):
            nc.gpsimd.memset(minus_half[:, :], -0.5)
            nc.gpsimd.memset(eps[:, :], EPS)
            nc.gpsimd.memset(ident[:, :], 0.0).then_inc(ident_zero, 1)
            pool.wait_ge(ident_zero, 1)
            nc.gpsimd.affine_select(out=ident[:, :], in_=ident[:, :], compare_op=ALU.not_equal, fill=1.0,
                                    base=0, pattern=[[-1, P]], channel_multiplier=1).then_inc(ident_ready, 1)

            def group(i, s):
                pool.wait_ge(var_ready, by_group(i, s))
                nc.gpsimd.tensor_tensor(rstd[s][:, :], mean_var[s][:, :, 1], eps[:, :], ALU.add
                                        ).then_inc(var_eps, 1)
                pool.wait_ge(var_eps, by_group(i, s))
                nc.gpsimd.tensor_tensor(rstd[s][:, :], rstd[s][:, :], minus_half[:, :], ALU.pow
                                        ).then_inc(rstd_ready, 1)

            with pool.Fori(0, ITERS) as i:
                for s in range(STREAMS):
                    group(i, s)


def kernel(**inputs):
    import numpy as np
    import concourse.bacc as bacc
    from concourse.bass_utils import run_bass_kernel_spmd

    x, adj = np.asarray(inputs["x"]), np.asarray(inputs["adj"])
    B, N, D = x.shape
    G, C = B // GB, D // P

    def w(name):
        a = np.asarray(inputs[f"L0_gnn_{name}_w"]).T
        return np.ascontiguousarray(a.reshape(-1, P, D).transpose(1, 0, 2).reshape(P, -1))

    b = np.stack([np.asarray(inputs[f"L0_gnn_{n}_b"]) for n in ("w3", "w4", "w5", "u3", "u5")])
    groups = x.reshape(G, GB, N, D)
    arrays = {
        "x_tok": np.ascontiguousarray(groups.transpose(0, 2, 1, 3).reshape(G, N, GB * D)),
        "x_feat": np.ascontiguousarray(
            groups.reshape(G, GB, N, C, P).transpose(0, 4, 3, 1, 2).reshape(G, P, C * GB * N)),
        "adj_t": np.ascontiguousarray(adj.T),
        "w3_t": w("w3"), "w4_t": w("w4"), "w5_t": w("w5"), "u3_t": w("u3"), "u5_t": w("u5"),
        "biases": np.ascontiguousarray(b.reshape(5, C, P).transpose(2, 0, 1).reshape(P, 5 * C)),
    }
    nc = bacc.Bacc("TRN2", target_bir_lowering=False, num_devices=1)
    args = [nc.dram_tensor(n, a.shape, mybir.dt.from_np(a.dtype), kind="ExternalInput").ap()
            for n, a in arrays.items()]
    out = nc.dram_tensor("out", (G, N, GB * D), F32, kind="ExternalOutput").ap()
    gated_graph_kernel(nc, *args, out)
    got = run_bass_kernel_spmd(nc, [arrays], core_ids=[0]).results[0]["out"]
    return got.reshape(G, N, GB, D).transpose(0, 2, 1, 3).reshape(B, N, D)
```

```python
from contextlib import ExitStack

import concourse.bass as bass
from concourse import mybir

P = 128
F32 = mybir.dt.float32
F32R = mybir.dt.float32r
ALU = mybir.AluOpType
ACT = mybir.ActivationFunctionType

T = 3
GB = 4
EPS = 1e-5


def gated_graph_kernel(nc, x_tok, x_feat, adj_t, w3_t, w4_t, w5_t, u3_t, u5_t, biases, out):
    GROUPS = x_tok.shape[0]
    N = adj_t.shape[0]
    D = x_tok.shape[2] // GB
    C = D // P
    TOK = GB * N
    assert N == P and C == 2 and TOK == 512
    STREAMS = 2
    ITERS = GROUPS // STREAMS
    SLOTS = STREAMS * T
    REG = STREAMS * (T - 1)
    PASSES = ((0, 0), (0, 1), (1, 0))

    with ExitStack() as ctx:
        def sb(name, shape, dt=F32):
            return ctx.enter_context(nc.sbuf_tensor(name, shape, dt))

        def sem(name):
            return ctx.enter_context(nc.semaphore(name))

        adj = sb("adj", [P, N])
        raw = {n: sb(f"raw_{n}", [P, 2 * C, D]) for n in ("w3", "w4", "w5")}
        raw |= {n: sb(f"raw_{n}", [P, C, D]) for n in ("u3", "u5")}
        wt = {n: sb(f"{n}_parts", [P, 2, C, D], F32R) for n in ("u3", "w4", "w3", "w5", "u5")}
        bias_in = sb("bias_in", [P, 5, C])
        gate_bias = sb("gate_bias", [P, 3, C])
        ident = sb("ident", [P, P])
        zero = sb("zero", [P, 1])
        table_first = sb("table_first", [P, 1])
        minus_half = sb("minus_half", [P, GB])
        eps = sb("eps", [P, GB])

        x_in = [sb(f"x_in{s}", [P, GB, D]) for s in range(STREAMS)]
        tok = [sb(f"tok{s}", [P, GB, D]) for s in range(STREAMS)]
        h0 = [sb(f"h0_{s}", [P, C, TOK]) for s in range(STREAMS)]
        h = [sb(f"h{s}", [P, C, TOK]) for s in range(STREAMS)]
        feat = [sb(f"feat{s}", [P, 2, C, TOK], F32R) for s in range(STREAMS)]
        y = [sb(f"y{s}", [P, GB, D]) for s in range(STREAMS)]
        stats = [sb(f"stats{s}", [P, GB, 6]) for s in range(STREAMS)]
        mean_var = [sb(f"mean_var{s}", [P, GB, 2]) for s in range(STREAMS)]
        rstd = [sb(f"rstd{s}", [P, GB]) for s in range(STREAMS)]

        a = sb("a", [P, 2, C, TOK], F32R)
        u = sb("u", [P, C, TOK])
        r = sb("r", [P, C, TOK])
        rh = sb("rh", [P, 2, C, TOK], F32R)
        z = sb("z", [P, C, TOK])
        cand = sb("cand", [P, C, TOK])

        ps_a = ctx.enter_context(nc.psum_tensor("ps_a", [P, C, TOK], F32))
        ps_r = ctx.enter_context(nc.psum_tensor("ps_r", [P, C, TOK], F32))
        ps_z = ctx.enter_context(nc.psum_tensor("ps_z", [P, C, TOK], F32))
        ps_c = ctx.enter_context(nc.psum_tensor("ps_c", [P, C, TOK], F32))

        adj_in = sem("adj_in")
        w_in = {n: sem(f"{n}_in") for n in ("u3", "w4", "w3", "w5", "u5")}
        b_in = sem("b_in")
        x_loaded = [sem(f"x_loaded{s}") for s in range(STREAMS)]
        h0_loaded = [sem(f"h0_loaded{s}") for s in range(STREAMS)]
        stored = [sem(f"stored{s}") for s in range(STREAMS)]
        w_ready = sem("w_ready")
        w_chain = sem("w_chain")
        bias_ready = sem("bias_ready")
        ident_zero = sem("ident_zero")
        ident_ready = sem("ident_ready")
        a_done = sem("a_done")
        u_done = sem("u_done")
        r_done = sem("r_done")
        z_done = sem("z_done")
        t_done = sem("t_done")
        c_done = sem("c_done")
        tanh_done = sem("tanh_done")
        a_hi_done = sem("a_hi_done")
        u_copied = sem("u_copied")
        r_sig = sem("r_sig")
        rh_hi_done = sem("rh_hi_done")
        z_sig = sem("z_sig")
        feat_hi_done = sem("feat_hi_done")
        tok_copied = sem("tok_copied")
        y_copied = sem("y_copied")
        h0_hi_done = sem("h0_hi_done")
        a_lo_done = sem("a_lo_done")
        rh_done = sem("rh_done")
        rh_lo_done = sem("rh_lo_done")
        z_added = sem("z_added")
        diff_done = sem("diff_done")
        step_done = sem("step_done")
        h_done = sem("h_done")
        feat_lo_done = sem("feat_lo_done")
        h0_lo_done = sem("h0_lo_done")
        last_h = sem("last_h")
        stats_done = sem("stats_done")
        var_ready = sem("var_ready")
        var_eps = sem("var_eps")
        rstd_ready = sem("rstd_ready")
        norm_done = sem("norm_done")
        end_step = sem("end_step")
        end_h_done = sem("end_h_done")

        def by_slot(i, k, c):
            return i * (C * SLOTS) + (C * k + c + 1)

        def once_by_slot(i, k):
            return i * SLOTS + (k + 1)

        def by_fed(i, k, c):
            return i * (C * REG) + (C * k + c + 1)

        def by_group(i, s, each=1):
            return i * (STREAMS * each) + each * (s + 1)

        def before(i, k):
            if k:
                return i, k - 1
            return None if isinstance(i, int) and i == 0 else (i - 1, SLOTS - 1)

        def after(i, k):
            return (i, k + 1) if k < SLOTS - 1 else (i + 1, 0)

        def where(k):
            return k % STREAMS, k // STREAMS

        def h_of(k):
            s, t = where(k)
            return h0[s] if t == 0 else h[s]

        block = ctx.enter_context(nc.Block())

        @block.sync
        def _(sp):
            def load_x(g, s):
                sp.dma_start(x_in[s][:, :, :], x_tok[g].rearrange("p (b d) -> p b d", b=GB)
                             ).then_inc(x_loaded[s], 16)

            def load_h0(g, s):
                sp.dma_start(h0[s][:, :, :], x_feat[g].rearrange("p (c t) -> p c t", c=C)
                             ).then_inc(h0_loaded[s], 16)

            def store_y(i, s):
                sp.wait_ge(norm_done, by_group(i, s))
                sp.dma_start(out[i * STREAMS + s].rearrange("p (b d) -> p b d", b=GB), y[s][:, :, :]
                             ).then_inc(stored[s], 16)

            def iteration(i, first, last):
                if not first:
                    sp.wait_ge(h_done, i * SLOTS)
                    load_h0(i * STREAMS + 1, 1)
                    store_y(i - 1, 0)
                    store_y(i - 1, 1)
                if not last:
                    for s in range(STREAMS):
                        sp.wait_ge(a_done, by_slot(i, s, 1))
                        load_x((i + 1) * STREAMS + s, s)
                    sp.wait_ge(h_done, once_by_slot(i, SLOTS - 2))
                    load_h0((i + 1) * STREAMS, 0)

            sp.dma_start(adj[:, :], adj_t).then_inc(adj_in, 16)
            load_x(0, 0)
            sp.dma_start(raw["w4"][:, :, :], w4_t.rearrange("p (c o) -> p c o", o=D)).then_inc(w_in["w4"], 16)
            sp.dma_start(raw["w5"][:, :, :], w5_t.rearrange("p (c o) -> p c o", o=D)).then_inc(w_in["w5"], 16)
            load_h0(1, 1)
            load_x(1, 1)
            iteration(0, True, False)
            with sp.Fori(1, ITERS - 1) as i:
                iteration(i, False, False)
            iteration(ITERS - 1, False, True)
            for s in range(STREAMS):
                store_y(ITERS - 1, s)
            for s in range(STREAMS):
                sp.wait_ge(stored[s], 16 * ITERS)


        @block.tensor
        def _(pe):
            def gate(ps, o, name, parts, begin, end, k_first=0):
                last = None
                for c in range(C):
                    for n, (w, d) in enumerate(PASSES):
                        last = pe.matmul(ps[:, o, :], wt[name][:, w, c, o * P:(o + 1) * P],
                                         parts[:, d, c, :],
                                         start=begin and c == 0 and n == 0,
                                         stop=end and c == C - 1 and n == len(PASSES) - 1,
                                         skip_group_check=True)
                return last

            def transpose_result(q, end=False):
                qi, qk = q
                s, _ = where(qk)
                if not end:
                    pe.wait_ge(h_done, once_by_slot(qi, qk))
                for j in range(2):
                    if end:
                        pe.wait_ge(end_h_done, j + 1)
                    for b in range(GB // 2 * j, GB // 2 * (j + 1)):
                        for c in range(C):
                            col = (b % (GB // 2)) * D + c * P
                            last = pe.transpose(ps_a[:, j, col:col + P], h[s][:, c, b * N:(b + 1) * N],
                                                ident[:, :])
                    last.then_inc(t_done, 1)

            def aggregate(i, k):
                s, t = where(k)
                started = not (isinstance(i, int) and i == 0)
                if t == 0:
                    pe.wait_ge(x_loaded[s], i * 16 + 16)
                state = x_in[s] if t == 0 else tok[s]
                for c in range(C):
                    if t == 0 and started:
                        pe.wait_ge(y_copied, by_group(i - 1, s, C) - (C - 1 - c))
                    for b in range(GB):
                        if t > 0 and c == 0 and b % (GB // 2) == 0:
                            pe.wait_ge(tok_copied, by_fed(i, k - STREAMS, b // (GB // 2)))
                        mm = pe.matmul(ps_a[:, c, b * N:(b + 1) * N], state[:, b, c * P:(c + 1) * P],
                                       adj[:, :], start=True, stop=True)
                    mm.then_inc(a_done, 1)

            def slot(i, k, first, last):
                s, t = where(k)
                start_up = first and k == 0
                if t == 0:
                    pe.wait_ge(h0_lo_done, by_group(i, s, C))
                else:
                    pe.wait_ge(feat_lo_done, by_fed(i, k - STREAMS, 1))
                if start_up:
                    pe.wait_ge(w_ready, 1)
                for o in range(C):
                    if not start_up:
                        pe.wait_ge(r_sig, by_slot(*before(i, k), o))
                    gate(ps_r, o, "u3", feat[s], True, False).then_inc(u_done, 1)
                pe.wait_ge(a_lo_done, by_slot(i, k, 1))
                if start_up:
                    pe.wait_ge(w_ready, 2)
                for o in range(C):
                    pe.wait_ge(u_copied, by_slot(i, k, o))
                    gate(ps_r, o, "w4", a, False, True).then_inc(r_done, 1)
                if start_up:
                    pe.wait_ge(w_ready, 3)
                for o in range(C):
                    if not start_up:
                        pe.wait_ge(z_sig, by_slot(*before(i, k), o))
                    gate(ps_z, o, "w3", a, True, True).then_inc(z_done, 1)
                if not start_up:
                    transpose_result(before(i, k))
                if start_up:
                    pe.wait_ge(w_ready, 4)
                for o in range(C):
                    if not start_up:
                        pe.wait_ge(tanh_done, by_slot(*before(i, k), o))
                    gate(ps_c, o, "w5", a, True, False)
                if not (last and k == SLOTS - 1):
                    aggregate(*after(i, k))
                if start_up:
                    pe.wait_ge(w_ready, 5)
                pe.wait_ge(rh_lo_done, by_slot(i, k, 1))
                for o in range(C):
                    gate(ps_c, o, "u5", rh, False, True).then_inc(c_done, 1)

            pe.wait_ge(adj_in, 16)
            aggregate(0, 0)
            pe.wait_ge(ident_ready, 1)
            for k in range(SLOTS):
                slot(0, k, True, False)
            with nc.Fori(1, ITERS - 1, engines=(mybir.EngineType.PE,), hint_back_edge=True) as i:
                for k in range(SLOTS):
                    slot(i, k, False, False)
            for k in range(SLOTS):
                slot(ITERS - 1, k, False, True)
            transpose_result((ITERS - 1, SLOTS - 1), end=True)

        @block.scalar
        def _(act):
            def tanh(q):
                qi, qk = q
                for o in range(C):
                    act.wait_ge(c_done, by_slot(qi, qk, o))
                    nc.scalar.activation(cand[:, o, :], ps_c[:, o, :], ACT.Tanh,
                                         bias=gate_bias[:, 2, o:o + 1]).then_inc(tanh_done, 1)

            def copy_y(q):
                qi, qk = q
                s, _ = where(qk)
                if not (isinstance(qi, int) and qi == 0):
                    act.wait_ge(stored[s], qi * 16)
                for j in range(2):
                    act.wait_ge(t_done, by_slot(qi, qk, j))
                    half = slice(GB // 2 * j, GB // 2 * (j + 1))
                    nc.scalar.activation(y[s][:, half, :], ps_a[:, j, :].rearrange("p (b d) -> p b d", d=D),
                                         ACT.Copy).then_inc(y_copied, 1)

            def split_a(i, k):
                for c in range(C):
                    act.wait_ge(a_done, by_slot(i, k, c))
                    nc.scalar.activation(a[:, 0, c, :], ps_a[:, c, :], ACT.Copy).then_inc(a_hi_done, 1)

            def split_h0(i, s):
                act.wait_ge(h0_loaded[s], i * 16 + 16)
                for c in range(C):
                    nc.scalar.activation(feat[s][:, 0, c, :], h0[s][:, c, :], ACT.Copy).then_inc(h0_hi_done, 1)

            def slot(i, k, first, last):
                q = before(i, k)
                if q:
                    tanh(q)
                    qs, qt = where(q[1])
                for o in range(C):
                    act.wait_ge(u_done, by_slot(i, k, o))
                    nc.scalar.activation(u[:, o, :], ps_r[:, o, :], ACT.Copy).then_inc(u_copied, 1)
                if q:
                    act.wait_ge(rh_lo_done, by_slot(*q, 1))
                for o in range(C):
                    act.wait_ge(r_done, by_slot(i, k, o))
                    nc.scalar.activation(r[:, o, :], ps_r[:, o, :], ACT.Sigmoid,
                                         bias=gate_bias[:, 1, o:o + 1]).then_inc(r_sig, 1)
                    if q:
                        act.wait_ge(h_done, once_by_slot(*q))
                        if qt < T - 1:
                            nc.scalar.activation(feat[qs][:, 0, o, :], h[qs][:, o, :], ACT.Copy
                                                 ).then_inc(feat_hi_done, 1)
                for c in range(C):
                    act.wait_ge(rh_done, by_slot(i, k, c))
                    nc.scalar.activation(rh[:, 0, c, :], r[:, c, :], ACT.Copy).then_inc(rh_hi_done, 1)
                if q and qt < T - 1:
                    for j in range(2):
                        act.wait_ge(t_done, by_slot(*q, j))
                        half = slice(GB // 2 * j, GB // 2 * (j + 1))
                        nc.scalar.activation(tok[qs][:, half, :],
                                             ps_a[:, j, :].rearrange("p (b d) -> p b d", d=D), ACT.Copy
                                             ).then_inc(tok_copied, 1)
                elif q:
                    copy_y(q)
                for o in range(C):
                    act.wait_ge(z_added, by_slot(i, k, o))
                    nc.scalar.activation(z[:, o, :], ps_z[:, o, :], ACT.Sigmoid,
                                         bias=gate_bias[:, 0, o:o + 1]).then_inc(z_sig, 1)
                if k == SLOTS - 1 and not last:
                    split_h0(i + 1, 0)
                if k == 0:
                    split_h0(i, 1)
                if not (last and k == SLOTS - 1):
                    split_a(*after(i, k))

            act.dma_start(raw["u3"][:, :, :], u3_t.rearrange("p (c o) -> p c o", o=D)).then_inc(w_in["u3"], 16)
            act.dma_start(h0[0][:, :, :], x_feat[0].rearrange("p (c t) -> p c t", c=C)).then_inc(h0_loaded[0], 16)
            act.dma_start(bias_in[:, :, :], biases.rearrange("p (n c) -> p n c", c=C)).then_inc(b_in, 16)
            act.dma_start(raw["w3"][:, :, :], w3_t.rearrange("p (c o) -> p c o", o=D)).then_inc(w_in["w3"], 16)
            act.dma_start(raw["u5"][:, :, :], u5_t.rearrange("p (c o) -> p c o", o=D)).then_inc(w_in["u5"], 16)
            act.wait_ge(ident_zero, 1)
            nc.scalar.activation(table_first[:, :], zero[:, :], ACT.Sigmoid)
            split_h0(0, 0)
            split_a(0, 0)
            act.wait_ge(bias_ready, 1)
            for k in range(SLOTS):
                slot(0, k, True, False)
            with nc.Fori(1, ITERS - 1, engines=(mybir.EngineType.Activation,), hint_back_edge=True) as i:
                for k in range(SLOTS):
                    slot(i, k, False, False)
            for k in range(SLOTS):
                slot(ITERS - 1, k, False, True)
            tanh((ITERS - 1, SLOTS - 1))
            copy_y((ITERS - 1, SLOTS - 1))

        @block.vector
        def _(dve):
            def lo(out_, full, hi):
                return nc.vector.tensor_tensor(out_, full, hi.bitcast(F32), ALU.subtract)

            chain = [0]

            def link(ins):
                chain[0] += 1
                ins.then_inc(w_chain, 1)
                dve.wait_ge(w_chain, chain[0])

            def prepare(name):
                dve.wait_ge(w_in[name], 16)
                w = raw[name]
                if name[0] == "w":
                    link(nc.vector.tensor_tensor(w[:, 0:C, :], w[:, 0:C, :], w[:, C:2 * C, :], ALU.add))
                link(nc.vector.tensor_copy(wt[name][:, 0, :, :], w[:, 0:C, :]))
                lo(wt[name][:, 1, :, :], w[:, 0:C, :], wt[name][:, 0, :, :]).then_inc(w_ready, 1)

            def split_h0(i, s):
                for c in range(C):
                    dve.wait_ge(h0_hi_done, by_group(i, s, C) - (C - 1 - c))
                    lo(feat[s][:, 1, c, :], h0[s][:, c, :], feat[s][:, 0, c, :]).then_inc(h0_lo_done, 1)

            def split_a(i, k):
                for c in range(C):
                    dve.wait_ge(a_hi_done, by_slot(i, k, c))
                    lo(a[:, 1, c, :], ps_a[:, c, :], a[:, 0, c, :]).then_inc(a_lo_done, 1)

            def diff(q):
                dve.wait_ge(tanh_done, by_slot(*q, 1))
                nc.vector.tensor_tensor(cand[:, :, :], cand[:, :, :], h_of(q[1])[:, :, :], ALU.subtract
                                        ).then_inc(diff_done, 1)

            def scale_by_z(q):
                dve.wait_ge(z_sig, by_slot(*q, 1))
                dve.wait_ge(diff_done, once_by_slot(*q))
                nc.vector.tensor_tensor(cand[:, :, :], cand[:, :, :], z[:, :, :], ALU.mult
                                        ).then_inc(step_done, 1)

            def new_h(q):
                qi, qk = q
                s, t = where(qk)
                dve.wait_ge(step_done, once_by_slot(*q))
                ins = nc.vector.tensor_tensor(h[s][:, :, :], cand[:, :, :], h_of(qk)[:, :, :], ALU.add)
                if t == T - 1:
                    ins.then_inc(last_h, 1)
                    dve.wait_ge(last_h, by_group(qi, s))
                    ins = nc.vector.tensor_tensor(h[s][:, :, :], h[s][:, :, :], h0[s][:, :, :], ALU.add)
                ins.then_inc(h_done, 1)

            def norm_stats(i, s):
                for b in range(GB):
                    if b % (GB // 2) == 0:
                        dve.wait_ge(y_copied, by_group(i, s, 2) - (1 - b // (GB // 2)))
                    ins = nc.vector.bn_stats(stats[s][:, b, :], y[s][:, b, :])
                ins.then_inc(stats_done, 1)

            def mean_and_var(i, s):
                for b in range(GB):
                    ins = nc.vector.bn_aggr(mean_var[s][:, b, :], stats[s][:, b, :])
                ins.then_inc(var_ready, 1)

            def normalise(i, s):
                dve.wait_ge(rstd_ready, by_group(i, s))
                for b in range(GB):
                    ins = nc.vector.tensor_scalar(y[s][:, b, :], y[s][:, b, :], mean_var[s][:, b, 0:1],
                                                  rstd[s][:, b:b + 1], ALU.subtract, ALU.mult)
                ins.then_inc(norm_done, 1)

            def slot(i, k, first, last):
                s, _ = where(k)
                q = before(i, k)
                if q:
                    if k < STREAMS and not first:
                        dve.wait_ge(stats_done, by_group(i - 1, k))
                    diff(q)
                    qs, qt = where(q[1])
                    if k < STREAMS and not first:
                        mean_and_var(i - 1, k)
                if q:
                    scale_by_z(q)
                    new_h(q)
                for c in range(C):
                    dve.wait_ge(r_sig, by_slot(i, k, c))
                    nc.vector.tensor_tensor(r[:, c, :], r[:, c, :], h_of(k)[:, c, :], ALU.mult
                                            ).then_inc(rh_done, 1)
                if q and qt < T - 1:
                    for c in range(C):
                        dve.wait_ge(feat_hi_done, by_fed(*q, c))
                        lo(feat[qs][:, 1, c, :], h[qs][:, c, :], feat[qs][:, 0, c, :]).then_inc(feat_lo_done, 1)
                for c in range(C):
                    dve.wait_ge(rh_hi_done, by_slot(i, k, c))
                    lo(rh[:, 1, c, :], r[:, c, :], rh[:, 0, c, :]).then_inc(rh_lo_done, 1)
                if k == 0 and not first:
                    normalise(i - 1, 0)
                if k == 1 and not first:
                    normalise(i - 1, 1)
                for o in range(C):
                    dve.wait_ge(z_done, by_slot(i, k, o))
                    dve.wait_ge(u_copied, by_slot(i, k, o))
                    nc.vector.tensor_tensor(ps_z[:, o, :], ps_z[:, o, :], u[:, o, :], ALU.add
                                            ).then_inc(z_added, 1)
                if k == SLOTS - 1 and not last:
                    split_h0(i + 1, 0)
                if k == 0:
                    split_h0(i, 1)
                if not (last and k == SLOTS - 1):
                    split_a(*after(i, k))
                if k == SLOTS - 1:
                    norm_stats(i, 0)
                if k == 0 and not first:
                    norm_stats(i - 1, 1)

            prepare("u3")
            split_h0(0, 0)
            prepare("w4")
            split_a(0, 0)
            dve.wait_ge(b_in, 16)
            for n, other in ((0, 3), (1, 3), (2, 4)):
                ins = nc.vector.tensor_tensor(gate_bias[:, n, :], bias_in[:, n, :], bias_in[:, other, :], ALU.add)
            ins.then_inc(bias_ready, 1)
            prepare("w3")
            prepare("w5")
            prepare("u5")
            for k in range(SLOTS):
                slot(0, k, True, False)
            with nc.Fori(1, ITERS - 1, engines=(mybir.EngineType.DVE,), hint_back_edge=True) as i:
                for k in range(SLOTS):
                    slot(i, k, False, False)
            for k in range(SLOTS):
                slot(ITERS - 1, k, False, True)
            end = (ITERS - 1, SLOTS - 1)
            dve.wait_ge(stats_done, by_group(ITERS - 1, 0))
            mean_and_var(ITERS - 1, 0)
            normalise(ITERS - 1, 0)
            halves = [slice(TOK // 2 * j, TOK // 2 * (j + 1)) for j in range(2)]
            dve.wait_ge(tanh_done, by_slot(*end, 1))
            dve.wait_ge(z_sig, by_slot(*end, 1))
            for t in halves:
                nc.vector.tensor_tensor(cand[:, :, t], cand[:, :, t], h[1][:, :, t], ALU.subtract
                                        ).then_inc(end_step, 1)
            for j, t in enumerate(halves):
                dve.wait_ge(end_step, j + 1)
                nc.vector.tensor_tensor(cand[:, :, t], cand[:, :, t], z[:, :, t], ALU.mult
                                        ).then_inc(end_step, 1)
            for j, t in enumerate(halves):
                dve.wait_ge(end_step, j + 3)
                nc.vector.tensor_tensor(h[1][:, :, t], h[1][:, :, t], cand[:, :, t], ALU.add
                                        ).then_inc(end_step, 1)
            for j, t in enumerate(halves):
                dve.wait_ge(end_step, j + 5)
                nc.vector.tensor_tensor(h[1][:, :, t], h[1][:, :, t], h0[1][:, :, t], ALU.add
                                        ).then_inc(end_h_done, 1)
            norm_stats(ITERS - 1, 1)
            dve.wait_ge(stats_done, by_group(ITERS - 1, 1))
            mean_and_var(ITERS - 1, 1)
            normalise(ITERS - 1, 1)

        @block.gpsimd
        def _(pool):
            nc.gpsimd.memset(minus_half[:, :], -0.5)
            nc.gpsimd.memset(eps[:, :], EPS)
            nc.gpsimd.memset(zero[:, :], 0.0)
            nc.gpsimd.memset(ident[:, :], 0.0).then_inc(ident_zero, 1)
            pool.wait_ge(ident_zero, 1)
            nc.gpsimd.affine_select(out=ident[:, :], in_=ident[:, :], compare_op=ALU.not_equal, fill=1.0,
                                    base=0, pattern=[[-1, P]], channel_multiplier=1).then_inc(ident_ready, 1)

            def group(i, s):
                pool.wait_ge(var_ready, by_group(i, s))
                nc.gpsimd.tensor_tensor(rstd[s][:, :], mean_var[s][:, :, 1], eps[:, :], ALU.add
                                        ).then_inc(var_eps, 1)
                pool.wait_ge(var_eps, by_group(i, s))
                nc.gpsimd.tensor_tensor(rstd[s][:, :], rstd[s][:, :], minus_half[:, :], ALU.pow
                                        ).then_inc(rstd_ready, 1)

            with pool.Fori(0, ITERS) as i:
                for s in range(STREAMS):
                    group(i, s)


def kernel(**inputs):
    import numpy as np
    import concourse.bacc as bacc
    from concourse.bass_utils import run_bass_kernel_spmd

    x, adj = np.asarray(inputs["x"]), np.asarray(inputs["adj"])
    B, N, D = x.shape
    G, C = B // GB, D // P

    def w(name):
        a = np.asarray(inputs[f"L0_gnn_{name}_w"]).T
        return np.ascontiguousarray(a.reshape(-1, P, D).transpose(1, 0, 2).reshape(P, -1))

    b = np.stack([np.asarray(inputs[f"L0_gnn_{n}_b"]) for n in ("w3", "w4", "w5", "u3", "u5")])
    groups = x.reshape(G, GB, N, D)
    arrays = {
        "x_tok": np.ascontiguousarray(groups.transpose(0, 2, 1, 3).reshape(G, N, GB * D)),
        "x_feat": np.ascontiguousarray(
            groups.reshape(G, GB, N, C, P).transpose(0, 4, 3, 1, 2).reshape(G, P, C * GB * N)),
        "adj_t": np.ascontiguousarray(adj.T),
        "w3_t": w("w3"), "w4_t": w("w4"), "w5_t": w("w5"), "u3_t": w("u3"), "u5_t": w("u5"),
        "biases": np.ascontiguousarray(b.reshape(5, C, P).transpose(2, 0, 1).reshape(P, 5 * C)),
    }
    nc = bacc.Bacc("TRN2", target_bir_lowering=False, num_devices=1)
    args = [nc.dram_tensor(n, a.shape, mybir.dt.from_np(a.dtype), kind="ExternalInput").ap()
            for n, a in arrays.items()]
    out = nc.dram_tensor("out", (G, N, GB * D), F32, kind="ExternalOutput").ap()
    gated_graph_kernel(nc, *args, out)
    got = run_bass_kernel_spmd(nc, [arrays], core_ids=[0]).results[0]["out"]
    return got.reshape(G, N, GB, D).transpose(0, 2, 1, 3).reshape(B, N, D)
```
